# Optimizing a Trainium2 kernel written in Bass

```python
import numpy as np
import jax
import jax.numpy as jnp

def _softmax(x, axis=-1):
    return jax.nn.softmax(x, axis=axis)

def _gelu(x):
    return jax.nn.gelu(x, approximate=True)

def _silu(x):
    return jax.nn.silu(x)

def _sigmoid(x):
    return jax.nn.sigmoid(x)

def _layernorm(x, axis=-1, eps=1e-05):
    m = jnp.mean(x, axis=axis, keepdims=True)
    v = jnp.var(x, axis=axis, keepdims=True)
    return (x - m) / jnp.sqrt(v + eps)

def _scatter_add(tgt, idx, src, axis=0):
    return tgt.at[idx].add(src)

def _segment_sum(src, seg, n):
    return jax.ops.segment_sum(src, seg, n)
kernel_name = 'mk_adj_resnorm_d1_adj_r2_537992'

def setup_inputs(seed: int=0):
    np.random.seed(seed)
    _w = jnp.asarray

    def _rec_inputs():
        import jax
        import jax.numpy as jnp
        _gk = jax.random.key(seed)
        x = -0.0002422 + 1 * jax.random.normal(jax.random.fold_in(_gk, 1), (128, 128, 512), jnp.float32)
        _a = jax.random.bernoulli(jax.random.fold_in(_gk, 2), 0.125, (128, 128, 128))
        adj = _a.astype(jnp.int32)
        return (x, adj)
    x, adj = _rec_inputs()

    def _L0_gnn_setup():
        import jax, jax.numpy as jnp
        import numpy as np
        IN_DIM = 512
        OUT_DIM = 512
        BATCH = 128
        NUM_OBJS = 100
        key = jax.random.key(seed)
        k1, k2, k3, k4, k5 = jax.random.split(key, 5)
        stdv = 1.0 / np.sqrt(OUT_DIM)
        feature = jax.random.normal(k1, (BATCH, NUM_OBJS, IN_DIM), dtype=jnp.float32)
        graph = jax.random.randint(k2, (BATCH, NUM_OBJS, NUM_OBJS), 0, 2, dtype=jnp.int32)
        weight = jax.random.uniform(k3, (IN_DIM, OUT_DIM), dtype=jnp.float32, minval=-stdv, maxval=stdv)
        wq = jax.random.uniform(k4, (IN_DIM, OUT_DIM), dtype=jnp.float32, minval=-stdv, maxval=stdv)
        wk = jax.random.uniform(k5, (IN_DIM, OUT_DIM), dtype=jnp.float32, minval=-stdv, maxval=stdv)
        return {'feature': feature, 'graph': graph, 'weight': weight, 'wq': wq, 'wk': wk}
    _L0_gnn_all = _L0_gnn_setup()
    _L0_gnn_in = {k: v for k, v in _L0_gnn_all.items() if k in ('weight', 'wq', 'wk')}
    del _L0_gnn_all
    return {'x': x, 'adj': adj, 'L0_gnn_weight': _L0_gnn_in['weight'], 'L0_gnn_wq': _L0_gnn_in['wq'], 'L0_gnn_wk': _L0_gnn_in['wk']}

def reference(x, adj, L0_gnn_weight, L0_gnn_wq, L0_gnn_wk):
    import jax
    import jax.numpy as jnp

    def _L0_gnn_ref(feature, graph, weight, wq, wk):
        import jax, jax.numpy as jnp
        import numpy as np
        IN_DIM = 512
        OUT_DIM = 512
        BATCH = 128
        NUM_OBJS = 100
        output = jnp.einsum('bni,io->bno', feature, weight)
        q = jnp.einsum('bni,io->bno', feature, wq)
        k = jnp.einsum('bni,io->bno', feature, wk)
        alpha = jnp.einsum('bno,bmo->bnm', q, k)
        alpha = jnp.maximum(alpha, 0.0) * (graph != 0).astype(alpha.dtype)
        alpha = jax.nn.softmax(alpha, axis=1)
        return jnp.einsum('bnm,bmo->bno', alpha, output)
    x = _layernorm(x + _L0_gnn_ref(x, adj, L0_gnn_weight, L0_gnn_wq, L0_gnn_wk), axis=-1)
    return x

_drawn_inputs = setup_inputs


def setup_inputs(seed=0):
    import zlib

    import numpy as np

    out = dict(_drawn_inputs(seed))
    spreads = {}
    factors = {}
    for name, (base, spread) in spreads.items():
        noise = np.random.default_rng([zlib.crc32(name.encode()), seed]).standard_normal(out[name].shape)
        drawn = base * np.exp(spread * noise) if base else spread * noise
        out[name] = jnp.asarray(drawn.astype(out[name].dtype))
    for name, factor in factors.items():
        out[name] = (out[name] * factor).astype(out[name].dtype)
    return out
```

```python
from contextlib import ExitStack

import concourse.bass as bass
from concourse import mybir

F32 = mybir.dt.float32
F32R = mybir.dt.float32r
I32 = mybir.dt.int32
ALU = mybir.AluOpType
ACT = mybir.ActivationFunctionType
AX_X = mybir.AxisListType.X

P = 128
G = 4
EPS = 1e-5


def graph_attention_layernorm(nc, xt, x, adjt, w, wqt, wkt, out):
    groups, _, chunks, cols = xt.shape
    nodes = x.shape[1]
    d = x.shape[2]
    assert nodes == P and chunks * P == d and cols == G * nodes and groups % 2 == 0
    banks_projection, banks_out = 3, 4
    rounds = groups // 2

    x_g = x.rearrange("(g b) n d -> g n b d", b=G)
    out_g = out.rearrange("(g b) n d -> g n b d", b=G)

    ctx = ExitStack()
    with ctx:
        def sb(name, shape, dt=F32):
            return ctx.enter_context(nc.sbuf_tensor(name, shape, dt))

        def sem(name):
            return ctx.enter_context(nc.semaphore(name))

        w_raw = sb("w_raw", [P, chunks, d])
        wqt_raw = sb("wqt_raw", [P, chunks, d])
        wkt_raw = sb("wkt_raw", [P, chunks, d])
        w_hi = sb("w_hi", [P, chunks, d], F32R)
        w_lo = sb("w_lo", [P, chunks, d], F32R)
        m_hi = sb("m_hi", [P, chunks, d], F32R)
        m_lo = sb("m_lo", [P, chunks, d], F32R)
        xt_in = [sb(f"xt_in{s}", [P, chunks, cols]) for s in range(2)]
        xt_hi = [sb(f"xt_hi{s}", [P, chunks, cols], F32R) for s in range(2)]
        xt_lo = [sb(f"xt_lo{s}", [P, chunks, cols], F32R) for s in range(2)]
        x_in = [sb(f"x_in{s}", [P, G, d]) for s in range(2)]
        adj_in = [sb(f"adj_in{s}", [P, cols], I32) for s in range(2)]
        result = x_in
        yt = sb("yt", [P, chunks, cols])
        v_hi = sb("v_hi", [P, G, d], F32R)
        v_lo = sb("v_lo", [P, G, d], F32R)
        masked = sb("masked", [P, cols])
        shifted = sb("shifted", [P, cols])
        expd = sb("expd", [P, cols])
        prob = sb("prob", [P, cols])
        p_hi = sb("p_hi", [P, cols], F32R)
        p_lo = sb("p_lo", [P, cols], F32R)
        row_max = sb("row_max", [P, G])
        row_sum = sb("row_sum", [P, G])
        row_inv = sb("row_inv", [P, G])
        stats = sb("stats", [P, G, 6])
        mean_gap, mean_sum, square_sum = sb("mean_gap", [P, G]), sb("mean_sum", [P, G]), sb("square_sum", [P, G])
        gap_term, square_term = sb("gap_term", [P, G]), sb("square_term", [P, G])
        mean = sb("mean", [P, G])
        var_eps = sb("var_eps", [P, G])
        minus_half = sb("minus_half", [P, G])
        rstd = sb("rstd", [P, G])

        proj = [ctx.enter_context(nc.psum_tensor(f"proj{i}", [P, d], F32)) for i in range(banks_projection)]
        alpha = ctx.enter_context(nc.psum_tensor("alpha", [P, cols], F32))
        attn = [ctx.enter_context(nc.psum_tensor(f"attn{i}", [P, d], F32)) for i in range(banks_out)]

        wq_loaded, wk_loaded, w_loaded = sem("wq_loaded"), sem("wk_loaded"), sem("w_loaded")
        xt_loaded = [sem(f"xt_loaded{s}") for s in range(2)]
        x_loaded = [sem(f"x_loaded{s}") for s in range(2)]
        adj_loaded = [sem(f"adj_loaded{s}") for s in range(2)]
        stored = [sem(f"stored{s}") for s in range(2)]
        m_done = sem("m_done")
        proj_done = sem("proj_done")
        alpha_done = sem("alpha_done")
        attn_done = sem("attn_done")
        m_hi_done, w_hi_done = sem("m_hi_done"), sem("w_hi_done")
        xt_hi_done = sem("xt_hi_done")
        yt_copied = sem("yt_copied")
        v_hi_done = sem("v_hi_done")
        exp_done = sem("exp_done")
        p_hi_done = sem("p_hi_done")
        m_split, w_split = sem("m_split"), sem("w_split")
        xt_split = sem("xt_split")
        v_split = sem("v_split")
        masked_done, max_done, clamp_done, shift_done = (
            sem("masked_done"), sem("max_done"), sem("clamp_done"), sem("shift_done"))
        sum_done, inv_done, prob_done, p_split = (
            sem("sum_done"), sem("inv_done"), sem("prob_done"), sem("p_split"))
        residual_done = sem("residual_done")
        stats_done = sem("stats_done")
        halves_added, terms_done = sem("halves_added"), sem("terms_done")
        var_done = sem("var_done")
        normalised = sem("normalised")
        half_set, rstd_done = sem("half_set"), sem("rstd_done")

        block = ctx.enter_context(nc.Block())

        @block.sync
        def _(sp):
            def load_xt(g, s):
                sp.dma_start(xt_in[s][:, :, :], xt[g, :, :, :]).then_inc(xt_loaded[s], 16)

            def load_adj(g, s):
                sp.dma_start(adj_in[s][:, :], adjt[g, :, :]).then_inc(adj_loaded[s], 16)

            def load_x(g, s):
                sp.dma_start(x_in[s][:, :, :], x_g[g, :, :, :]).then_inc(x_loaded[s], 16)

            def store(g, s):
                sp.wait_ge(normalised, g + 1)
                sp.dma_start(out_g[g, :, :, :], result[s][:, :, :]).then_inc(stored[s], 16)

            load_xt(0, 0)
            sp.dma_start(w_raw[:, :, :], w).then_inc(w_loaded, 16)
            load_adj(0, 0)
            load_x(0, 0)
            load_xt(1, 1)
            load_adj(1, 1)
            load_x(1, 1)
            with sp.Fori(0, rounds - 1) as r:
                for s in range(2):
                    g = r * 2 + s
                    sp.wait_ge(alpha_done, g + 1)
                    load_xt(g + 2, s)
                    sp.wait_ge(masked_done, g + 1)
                    load_adj(g + 2, s)
                    store(g, s)
                    sp.wait_ge(stored[s], (r + 1) * 16)
                    load_x(g + 2, s)
            for s in range(2):
                store(groups - 2 + s, s)
            for s in range(2):
                sp.wait_ge(stored[s], rounds * 16)

        @block.tensor
        def _(pe):
            def product(bank, pairs):
                for n, (lhs, rhs) in enumerate(pairs):
                    last = nc.tensor.matmul(bank, lhs, rhs, start=n == 0, stop=n == len(pairs) - 1)
                return last

            pe.wait_ge(wq_loaded, 16)
            pe.wait_ge(wk_loaded, 16)
            for i in range(chunks):
                product(attn[i][:, :], [(wqt_raw[:, o, i * P:(i + 1) * P], wkt_raw[:, o, :])
                                        for o in range(chunks)]).then_inc(m_done, 1)

            pe.wait_ge(m_split, chunks)
            with pe.Fori(0, rounds) as r:
                for s in range(2):
                    g = r * 2 + s
                    hi, lo = xt_hi[s], xt_lo[s]
                    pe.wait_ge(xt_split, (g + 1) * chunks)
                    for j in range(chunks):
                        c = slice(j * P, (j + 1) * P)
                        if j == banks_projection:
                            pe.wait_ge(yt_copied, g * chunks + 1)
                        pairs = []
                        for i in range(chunks):
                            pairs += [(m_hi[:, i, c], hi[:, i, :]), (m_hi[:, i, c], lo[:, i, :]),
                                      (m_lo[:, i, c], hi[:, i, :])]
                        product(proj[j % banks_projection][:, :], pairs).then_inc(proj_done, 1)

                    for b in range(G):
                        c = slice(b * P, (b + 1) * P)
                        k = chunks + b
                        if b == 0:
                            pe.wait_ge(yt_copied, g * chunks + 2)
                            if s == 0:
                                pe.wait_ge(w_split, 1)
                        if b == 3:
                            pe.wait_ge(v_split, g * G + 1)
                        pairs = []
                        for i in range(chunks):
                            pairs += [(hi[:, i, c], w_hi[:, i, :]), (hi[:, i, c], w_lo[:, i, :]),
                                      (lo[:, i, c], w_hi[:, i, :])]
                        product(proj[k % banks_projection][:, :], pairs).then_inc(proj_done, 1)
                        if b == 0:
                            pe.wait_ge(yt_copied, (g + 1) * chunks)
                            for a in range(G):
                                ca = slice(a * P, (a + 1) * P)
                                last = product(alpha[:, ca], [(xt_in[s][:, i, ca], yt[:, i, ca])
                                                              for i in range(chunks)])
                            last.then_inc(alpha_done, 1)

                    pe.wait_ge(p_split, g + 1)
                    for b in range(G):
                        c = slice(b * P, (b + 1) * P)
                        pe.wait_ge(v_split, g * G + b + 1)
                        product(attn[b][:, :], [(p_hi[:, c], v_hi[:, b, :]), (p_hi[:, c], v_lo[:, b, :]),
                                                (p_lo[:, c], v_hi[:, b, :])]).then_inc(attn_done, 1)

        @block.scalar
        def _(act):
            act.dma_start(wqt_raw[:, :, :], wqt).then_inc(wq_loaded, 16)
            act.dma_start(wkt_raw[:, :, :], wkt).then_inc(wk_loaded, 16)

            def split_xt(g, s, i):
                nc.scalar.copy(xt_hi[s][:, i, :], xt_in[s][:, i, :]).then_inc(xt_hi_done, 1)

            act.wait_ge(xt_loaded[0], 16)
            for i in range(chunks):
                split_xt(0, 0, i)
            act.wait_ge(w_loaded, 16)
            nc.scalar.copy(w_hi[:, :, :], w_raw[:, :, :]).then_inc(w_hi_done, 1)
            for i in range(chunks):
                act.wait_ge(m_done, i + 1)
                nc.scalar.copy(m_hi[:, i, :], attn[i][:, :]).then_inc(m_hi_done, 1)

            def group(r, s, ahead):
                g = r * 2 + s
                for j in range(chunks):
                    act.wait_ge(proj_done, g * 8 + j + 1)
                    nc.scalar.copy(yt[:, j, :], proj[j % banks_projection][:, :]).then_inc(yt_copied, 1)
                    if ahead:
                        if j == 0:
                            act.wait_ge(xt_loaded[1 - s], (r + 1 + s) * 16)
                        split_xt(g + 1, 1 - s, j)
                for b in range(G):
                    if b == 1:
                        act.wait_ge(shift_done, g + 1)
                        nc.scalar.activation(expd[:, :], shifted[:, :], ACT.Exp).then_inc(exp_done, 1)
                    if b == 2:
                        act.wait_ge(prob_done, g + 1)
                        nc.scalar.copy(p_hi[:, :], prob[:, :]).then_inc(p_hi_done, 1)
                    k = chunks + b
                    act.wait_ge(proj_done, g * 8 + k + 1)
                    nc.scalar.copy(v_hi[:, b, :], proj[k % banks_projection][:, :]).then_inc(v_hi_done, 1)

            with act.Fori(0, rounds - 1) as r:
                group(r, 0, True)
                group(r, 1, True)
            group(rounds - 1, 0, True)
            group(rounds - 1, 1, False)

        @block.vector
        def _(dve):
            def batches(t):
                return t[:, :].rearrange("p (b n) -> p b n", b=G)

            def over_n(t):
                return t[:, :].unsqueeze(2).to_broadcast([P, G, nodes])

            def split_xt(g, s, i):
                dve.wait_ge(xt_hi_done, g * chunks + i + 1)
                nc.vector.tensor_tensor(xt_lo[s][:, i, :], xt_in[s][:, i, :],
                                        xt_hi[s][:, i, :].bitcast(F32), ALU.subtract).then_inc(xt_split, 1)

            for i in range(chunks):
                split_xt(0, 0, i)
            dve.wait_ge(w_hi_done, 1)
            nc.vector.tensor_tensor(w_lo[:, :, :], w_raw[:, :, :], w_hi[:, :, :].bitcast(F32),
                                    ALU.subtract).then_inc(w_split, 1)
            for i in range(chunks):
                dve.wait_ge(m_hi_done, i + 1)
                nc.vector.tensor_tensor(m_lo[:, i, :], attn[i][:, :], m_hi[:, i, :].bitcast(F32),
                                        ALU.subtract).then_inc(m_split, 1)

            def split_v(g, b):
                dve.wait_ge(v_hi_done, g * G + b + 1)
                nc.vector.tensor_tensor(v_lo[:, b, :], proj[(chunks + b) % banks_projection][:, :],
                                        v_hi[:, b, :].bitcast(F32), ALU.subtract).then_inc(v_split, 1)

            def group(r, s, ahead):
                g = r * 2 + s
                if ahead:
                    for i in range(chunks):
                        split_xt(g + 1, 1 - s, i)
                split_v(g, 0)
                dve.wait_ge(adj_loaded[s], (r + 1) * 16)
                dve.wait_ge(alpha_done, g + 1)
                nc.vector.scalar_tensor_tensor(out=masked[:, :], in0=adj_in[s][:, :], scalar=0.0,
                                               in1=alpha[:, :], op0=ALU.not_equal,
                                               op1=ALU.mult).then_inc(masked_done, 1)
                dve.wait_ge(masked_done, g + 1)
                nc.vector.reduce_max(row_max[:, :], batches(masked), AX_X).then_inc(max_done, 1)
                dve.wait_ge(max_done, g + 1)
                nc.vector.tensor_scalar(row_max[:, :], row_max[:, :], 0.0, None, ALU.max).then_inc(clamp_done, 1)
                dve.wait_ge(clamp_done, g + 1)
                nc.vector.scalar_tensor_tensor(out=batches(shifted), in0=batches(masked), scalar=0.0,
                                               in1=over_n(row_max), op0=ALU.max,
                                               op1=ALU.subtract).then_inc(shift_done, 1)
                split_v(g, 1)
                dve.wait_ge(exp_done, g + 1)
                nc.vector.reduce_sum(row_sum[:, :], batches(expd), AX_X).then_inc(sum_done, 1)
                dve.wait_ge(sum_done, g + 1)
                nc.vector.reciprocal(row_inv[:, :], row_sum[:, :]).then_inc(inv_done, 1)
                dve.wait_ge(inv_done, g + 1)
                nc.vector.tensor_tensor(batches(prob), batches(expd), over_n(row_inv),
                                        ALU.mult).then_inc(prob_done, 1)
                split_v(g, 2)
                dve.wait_ge(p_hi_done, g + 1)
                nc.vector.tensor_tensor(p_lo[:, :], prob[:, :], p_hi[:, :].bitcast(F32),
                                        ALU.subtract).then_inc(p_split, 1)
                split_v(g, 3)

                def residual(b):
                    dve.wait_ge(attn_done, g * G + b + 1)
                    nc.vector.tensor_tensor(x_in[s][:, b, :], attn[b][:, :], x_in[s][:, b, :],
                                            ALU.add).then_inc(residual_done, 1)

                def statistics(b):
                    dve.wait_ge(residual_done, g * G + b + 1)
                    nc.vector.bn_stats(stats[:, b, :], x_in[s][:, b, :]).then_inc(stats_done, 1)

                dve.wait_ge(x_loaded[s], (r + 1) * 16)
                residual(0)
                for b in range(1, G):
                    residual(b)
                    statistics(b - 1)
                statistics(G - 1)
                mean_even, mean_odd = stats[:, :, 1], stats[:, :, 4]
                dve.wait_ge(stats_done, (g + 1) * G)
                nc.vector.tensor_tensor(mean_gap[:, :], mean_even, mean_odd, ALU.subtract)
                nc.vector.tensor_tensor(mean_sum[:, :], mean_even, mean_odd, ALU.add)
                nc.vector.tensor_tensor(square_sum[:, :], stats[:, :, 2], stats[:, :, 5], ALU.add).then_inc(halves_added, 1)
                dve.wait_ge(halves_added, g + 1)
                nc.vector.scalar_tensor_tensor(out=gap_term[:, :], in0=mean_gap[:, :], scalar=0.25,
                                               in1=mean_gap[:, :], op0=ALU.mult, op1=ALU.mult)
                nc.vector.tensor_scalar(mean[:, :], mean_sum[:, :], 0.5, None, ALU.mult)
                nc.vector.tensor_scalar(square_term[:, :], square_sum[:, :], 1.0 / d, EPS, ALU.mult,
                                        ALU.add).then_inc(terms_done, 1)
                dve.wait_ge(terms_done, g + 1)
                nc.vector.tensor_tensor(var_eps[:, :], square_term[:, :], gap_term[:, :], ALU.add).then_inc(var_done, 1)
                dve.wait_ge(rstd_done, g + 1)
                for b in range(G):
                    last = nc.vector.tensor_scalar(result[s][:, b, :], x_in[s][:, b, :],
                                                   mean[:, b:b + 1], rstd[:, b:b + 1],
                                                   ALU.subtract, ALU.mult)
                last.then_inc(normalised, 1)

            with dve.Fori(0, rounds - 1) as r:
                group(r, 0, True)
                group(r, 1, True)
            group(rounds - 1, 0, True)
            group(rounds - 1, 1, False)

        @block.gpsimd
        def _(pool):
            nc.gpsimd.memset(minus_half[:, :], -0.5).then_inc(half_set, 1)
            pool.wait_ge(half_set, 1)
            with pool.Fori(0, groups) as g:
                pool.wait_ge(var_done, g + 1)
                nc.gpsimd.tensor_tensor(rstd[:, :], var_eps[:, :], minus_half[:, :], ALU.pow).then_inc(rstd_done, 1)


def kernel(x, adj, L0_gnn_weight, L0_gnn_wq, L0_gnn_wk):
    import numpy as np
    import concourse.bacc as bacc
    from concourse.bass_utils import run_bass_kernel_spmd

    x, adj = np.asarray(x), np.asarray(adj)
    batch, nodes, d = x.shape
    groups, chunks = batch // G, d // P

    def rows_in_chunks(m):
        m = np.asarray(m)
        return np.ascontiguousarray(m.reshape(chunks, P, m.shape[1]).transpose(1, 0, 2))

    arrays = {
        "xt": np.ascontiguousarray(x.reshape(groups, G, nodes, chunks, P).transpose(0, 4, 3, 1, 2)
                                   ).reshape(groups, P, chunks, G * nodes),
        "x": np.ascontiguousarray(x),
        "adjt": np.ascontiguousarray(adj.reshape(groups, G, nodes, nodes).transpose(0, 3, 1, 2)
                                     ).reshape(groups, nodes, G * nodes),
        "w": rows_in_chunks(L0_gnn_weight),
        "wqt": rows_in_chunks(np.asarray(L0_gnn_wq).T),
        "wkt": rows_in_chunks(np.asarray(L0_gnn_wk).T),
    }
    nc = bacc.Bacc("TRN2", target_bir_lowering=False, num_devices=1)
    args = {k: nc.dram_tensor(f"in_{k}", a.shape, mybir.dt.from_np(a.dtype), kind="ExternalInput").ap()
            for k, a in arrays.items()}
    out = nc.dram_tensor("out_y", x.shape, F32, kind="ExternalOutput").ap()
    graph_attention_layernorm(nc, **args, out=out)
    r = run_bass_kernel_spmd(nc, [{f"in_{k}": a for k, a in arrays.items()}], core_ids=[0])
    return r.results[0]["out_y"]
```

```python
from contextlib import ExitStack

import concourse.bass as bass
from concourse import mybir

F32 = mybir.dt.float32
F32R = mybir.dt.float32r
BF16 = mybir.dt.bfloat16
I32 = mybir.dt.int32
ALU = mybir.AluOpType
ACT = mybir.ActivationFunctionType
AX_X = mybir.AxisListType.X

P = 128
G = 4
BANK = 512
EPS = 1e-5
WARM_UP = 16


def graph_attention_layernorm(nc, xt, x, adjt, w, wqt, wkt, out):
    groups, _, chunks, cols = xt.shape
    nodes = x.shape[1]
    d = x.shape[2]
    assert nodes == P and chunks * P == d == BANK and cols == G * nodes and G == chunks == 4
    assert groups % 2 == 0 and groups >= 6
    last_group = groups - 1
    half = (d + nodes) // 2
    w_tail = half - nodes
    v_from = BANK - half
    alpha_from = v_from + d

    x_g = x.rearrange("(g b) n d -> g n b d", b=G)
    out_g = out.rearrange("(g b) n d -> g n b d", b=G)

    ctx = ExitStack()
    with ctx:
        def sb(name, shape, dt=F32):
            return ctx.enter_context(nc.sbuf_tensor(name, shape, dt))

        def sem(name):
            return ctx.enter_context(nc.semaphore(name))

        w_raw = sb("w_raw", [P, chunks, d])
        wqt_raw = sb("wqt_raw", [P, chunks, d])
        wkt_raw = sb("wkt_raw", [P, chunks, d])
        m_hi = sb("m_hi", [P, chunks, d], F32R)
        m_lo = sb("m_lo", [P, chunks, d], F32R)
        w_hi = sb("w_hi", [P, chunks, half], F32R)
        w_lo = sb("w_lo", [P, chunks, half], F32R)
        wy_hi = sb("wy_hi", [P, chunks, G, half], F32R)
        wy_lo = sb("wy_lo", [P, chunks, G, half], F32R)
        xt_in = [sb(f"xt_in{s}", [P, chunks, cols]) for s in range(2)]
        xt_hi = [sb(f"xt_hi{s}", [P, chunks, cols], F32R) for s in range(2)]
        xt_lo = [sb(f"xt_lo{s}", [P, chunks, cols], F32R) for s in range(2)]
        x_in = [sb(f"x_in{s}", [P, G, d]) for s in range(2)]
        adj_in = [sb(f"adj_in{s}", [P, cols], I32) for s in range(2)]
        result = x_in
        v_hi = sb("v_hi", [P, G, d], F32R)
        v_lo = sb("v_lo", [P, G, d], F32R)
        masked = sb("masked", [P, cols])
        shifted = sb("shifted", [P, cols])
        expd = sb("expd", [P, cols])
        prob = sb("prob", [P, cols])
        p_hi = sb("p_hi", [P, cols], F32R)
        p_lo = sb("p_lo", [P, cols], F32R)
        row_max = sb("row_max", [P, G])
        row_sum = sb("row_sum", [P, G])
        row_inv = sb("row_inv", [P, G])
        stats = sb("stats", [P, G, 6])
        mean_gap, mean_sum, square_sum = sb("mean_gap", [P, G]), sb("mean_sum", [P, G]), sb("square_sum", [P, G])
        gap_term, square_term = sb("gap_term", [P, G]), sb("square_term", [P, G])
        minus_mean = sb("minus_mean", [P, G])
        var_eps = sb("var_eps", [P, G])
        minus_half = sb("minus_half", [P, G])
        rstd = sb("rstd", [P, G])
        offset = sb("offset", [P, G])
        ignored = sb("ignored", [P, G])
        zeros = sb("zeros", [P, BANK], BF16)
        wq_hi, wq_lo, wk_hi, wk_lo = v_hi, v_lo, xt_hi[1], xt_lo[1]

        pair = [ctx.enter_context(nc.psum_tensor(f"pair{i}", [P, 2 * BANK], F32)) for i in range(4)]
        bank = [pair[i // 2][:, (i % 2) * BANK:(i % 2 + 1) * BANK] for i in range(8)]
        v_of = [pair[b][:, v_from:alpha_from] for b in range(G)]
        alpha_of = [pair[b][:, alpha_from:alpha_from + nodes] for b in range(G)]

        def attended(g_is_last, b):
            return bank[b if g_is_last else 4 + b]

        wqk_loaded = [sem(f"wqk_loaded{o}") for o in range(chunks)]
        w_loaded = sem("w_loaded")
        xt_loaded = [sem(f"xt_loaded{s}") for s in range(2)]
        x_loaded = [sem(f"x_loaded{s}") for s in range(2)]
        adj_loaded = [sem(f"adj_loaded{s}") for s in range(2)]
        stored = [sem(f"stored{s}") for s in range(2)]
        m_done = sem("m_done")
        yt_done = sem("yt_done")
        v_done = sem("v_done")
        v_head_done = sem("v_head_done")
        attn_done = sem("attn_done")
        wqk_hi_done = sem("wqk_hi_done")
        m_hi_done, w_hi_done = sem("m_hi_done"), sem("w_hi_done")
        xt_hi_done = sem("xt_hi_done")
        y_hi_done = sem("y_hi_done")
        v_hi_done = sem("v_hi_done")
        v_head_hi_done = sem("v_head_hi_done")
        exp_done = sem("exp_done")
        p_hi_done = sem("p_hi_done")
        normalised = sem("normalised")
        wqk_split, m_split, w_split = sem("wqk_split"), sem("m_split"), sem("w_split")
        xt_split = sem("xt_split")
        y_split = sem("y_split")
        v_split = sem("v_split")
        v_head_split = sem("v_head_split")
        masked_done = sem("masked_done")
        max_done, clamp_done, shift_done = sem("max_done"), sem("clamp_done"), sem("shift_done")
        sum_done, inv_done, prob_done, p_split = (
            sem("sum_done"), sem("inv_done"), sem("prob_done"), sem("p_split"))
        residual_done = sem("residual_done")
        stats_done = sem("stats_done")
        halves_added, terms_done, var_done = sem("halves_added"), sem("terms_done"), sem("var_done")
        half_set, rstd_done, offset_done = sem("half_set"), sem("rstd_done"), sem("offset_done")
        zeros_set = sem("zeros_set")

        softmax_parts = [(0, 2), (2, 4)]
        norm_parts = [(0, 2), (2, 3), (3, 4)]

        block = ctx.enter_context(nc.Block())

        @block.sync
        def _(sp):
            def load_xt(g, s):
                sp.dma_start(xt_in[s][:, :, :], xt[g, :, :, :]).then_inc(xt_loaded[s], 16)

            def load_adj(g, s):
                sp.dma_start(adj_in[s][:, :], adjt[g, :, :]).then_inc(adj_loaded[s], 16)

            def load_x(g, s):
                sp.dma_start(x_in[s][:, :, :], x_g[g, :, :, :]).then_inc(x_loaded[s], 16)

            def group(g, s, use, next_xt=True):
                sp.wait_ge(masked_done, (g + 1) * G)
                load_adj(g + 2, s)
                if next_xt:
                    sp.wait_ge(xt_split, (g + 2) * chunks)
                    load_xt(g + 3, 1 - s)
                sp.wait_ge(normalised, g + 1)
                sp.dma_start(out_g[g, :, :, :], result[s][:, :, :]).then_inc(stored[s], 16)
                sp.wait_ge(stored[s], use * 16)
                load_x(g + 2, s)

            for o in range(chunks):
                sp.dma_start(wqt_raw[:, o, :], wqt[:, o, :]).then_inc(wqk_loaded[o], 16)
                if o >= 2:
                    sp.dma_start(wkt_raw[:, o, :], wkt[:, o, :]).then_inc(wqk_loaded[o], 16)
            load_xt(0, 0)
            sp.dma_start(w_raw[:, :, :], w).then_inc(w_loaded, 16)
            load_xt(1, 1)
            load_adj(0, 0)
            load_x(0, 0)
            load_adj(1, 1)
            load_x(1, 1)
            sp.wait_ge(xt_split, chunks)
            load_xt(2, 0)
            with sp.Fori(0, groups // 2 - 2) as r:
                group(r * 2, 0, r + 1)
                group(r * 2 + 1, 1, r + 1)
            group(last_group - 3, 0, groups // 2 - 1)
            group(last_group - 2, 1, groups // 2 - 1, next_xt=False)
            sp.wait_ge(normalised, last_group)
            sp.dma_start(out_g[last_group - 1, :, :, :], result[0][:, :, :]).then_inc(stored[0], 16)
            for n, (b0, b1) in enumerate(norm_parts):
                sp.wait_ge(normalised, last_group + n + 1)
                sp.dma_start(out_g[last_group, :, b0:b1, :], result[1][:, b0:b1, :]).then_inc(stored[1], 16)
            sp.wait_ge(stored[0], groups // 2 * 16)
            sp.wait_ge(stored[1], (groups // 2 - 1 + len(norm_parts)) * 16)

        @block.tensor
        def _(pe):
            pe.wait_ge(zeros_set, 1)
            for _ in range(WARM_UP):
                nc.tensor.matmul(bank[0], zeros[:, 0:P], zeros[:, :], start=True, stop=True)

            for o in range(chunks):
                pe.wait_ge(wqk_split, 2 * (o + 1))
                for i in range(chunks):
                    c = slice(i * P, (i + 1) * P)
                    terms = [(wq_hi, wk_hi), (wq_hi, wk_lo), (wq_lo, wk_hi)]
                    for n, (q, k) in enumerate(terms):
                        last = nc.tensor.matmul(bank[4 + i], q[:, o, c], k[:, o, :], start=o == n == 0,
                                                stop=o == chunks - 1 and n == len(terms) - 1)
                    if o == chunks - 1:
                        last.then_inc(m_done, 1)

            def attend(b, last_one=False):
                c = slice(b * P, (b + 1) * P)
                terms = [(p_hi, v_hi), (p_hi, v_lo), (p_lo, v_hi)]
                for n, (p, v) in enumerate(terms):
                    last = nc.tensor.matmul(attended(last_one, b), p[:, c], v[:, b, :],
                                            start=n == 0, stop=n == len(terms) - 1)
                last.then_inc(attn_done, 1)

            def group(g, s, first=False, last_one=False):
                hi, lo = xt_hi[s], xt_lo[s]
                pe.wait_ge(xt_split, (g + 1) * chunks)
                for j in range(chunks):
                    if not first and j in (0, 2):
                        pe.wait_ge(masked_done, (g - 1) * G + j // 2 + 1)
                    c = slice(j * P, (j + 1) * P)
                    for i in range(chunks):
                        if first and j == 0:
                            pe.wait_ge(m_split, i + 1)
                        terms = [(m_hi, hi), (m_hi, lo), (m_lo, hi)]
                        for n, (m, t) in enumerate(terms):
                            last = nc.tensor.matmul(bank[j], m[:, i, c], t[:, i, :], start=i == n == 0,
                                                    stop=i == chunks - 1 and n == len(terms) - 1)
                    last.then_inc(yt_done, 1)
                if not first:
                    pe.wait_ge(p_split, g)
                    for b in range(G):
                        attend(b)

                def head(b, i):
                    return (pair[b][:, v_from:BANK],
                            [(hi, w_hi[:, i, :]), (hi, w_lo[:, i, :]), (lo, w_hi[:, i, :])])

                def tail(b, i):
                    return (pair[b][:, BANK:BANK + half],
                            [(hi, wy_hi[:, i, b, :]), (hi, wy_lo[:, i, b, :]), (lo, wy_hi[:, i, b, :])])

                def multiply(b, halves):
                    for i in range(chunks):
                        if first and b == 0:
                            pe.wait_ge(y_split, max(i + 1, 2))
                        for n in range(3):
                            for columns in halves:
                                to, terms = columns(b, i)
                                t, wy = terms[n]
                                last = nc.tensor.matmul(to, t[:, i, b * P:(b + 1) * P], wy, start=i == n == 0,
                                                        stop=i == chunks - 1 and n == 2)
                    return last

                if first:
                    pe.wait_ge(w_split, 2)
                else:
                    pe.wait_ge(y_split, (g + 1) * chunks)
                for b in range(G):
                    if not first and b >= 2:
                        pe.wait_ge(residual_done, (g - 1) * G + (b - 1) * 2)
                    multiply(b, [tail] if last_one else [head, tail]).then_inc(v_done, 1)
                if last_one:
                    for b in range(G + 1):
                        if b < G:
                            multiply(b, [head]).then_inc(v_head_done, 1)
                        if b >= 1:
                            n = [b0 <= b - 1 < b1 for b0, b1 in softmax_parts].index(True)
                            pe.wait_ge(p_split, last_group + n + 1)
                            pe.wait_ge(v_head_split, b)
                            attend(b - 1, last_one=True)

            group(0, 0, first=True)
            with pe.Fori(0, groups // 2 - 1) as r:
                group(r * 2 + 1, 1)
                group(r * 2 + 2, 0)
            group(last_group, 1, last_one=True)

        @block.scalar
        def _(act):
            for o in range(2):
                act.dma_start(wkt_raw[:, o, :], wkt[:, o, :]).then_inc(wqk_loaded[o], 16)

            act.wait_ge(half_set, 1)
            nc.scalar.activation(ignored[:, :], minus_half[:, :], ACT.Exp)

            for o in range(chunks):
                act.wait_ge(wqk_loaded[o], 32)
                nc.scalar.copy(wq_hi[:, o, :], wqt_raw[:, o, :]).then_inc(wqk_hi_done, 1)
                nc.scalar.copy(wk_hi[:, o, :], wkt_raw[:, o, :]).then_inc(wqk_hi_done, 1)

            def split_xt(s, i):
                nc.scalar.copy(xt_hi[s][:, i, :], xt_in[s][:, i, :]).then_inc(xt_hi_done, 1)

            act.wait_ge(xt_loaded[0], 16)
            for i in range(chunks):
                split_xt(0, i)
            for i in range(chunks):
                act.wait_ge(m_done, i + 1)
                nc.scalar.copy(m_hi[:, i, :], bank[4 + i]).then_inc(m_hi_done, 1)
            act.wait_ge(w_loaded, 16)
            nc.scalar.copy(w_hi[:, :, :], w_raw[:, :, 0:half]).then_inc(w_hi_done, 1)
            for b in range(G):
                nc.scalar.copy(wy_hi[:, :, b, 0:w_tail], w_raw[:, :, half:d]).then_inc(w_hi_done, 1)

            def exponent(n, b0, b1):
                c = slice(b0 * P, b1 * P)
                act.wait_ge(shift_done, n)
                nc.scalar.activation(expd[:, c], shifted[:, c], ACT.Exp).then_inc(exp_done, 1)

            def split_p(n, b0, b1):
                c = slice(b0 * P, b1 * P)
                act.wait_ge(prob_done, n)
                nc.scalar.copy(p_hi[:, c], prob[:, c]).then_inc(p_hi_done, 1)

            def split_y(g, j):
                act.wait_ge(yt_done, g * chunks + j + 1)
                nc.scalar.copy(wy_hi[:, j, :, w_tail:half],
                               bank[j].rearrange("p (b n) -> p b n", b=G)).then_inc(y_hi_done, 1)

            def split_v(g, b):
                act.wait_ge(v_done, g * G + b + 1)
                nc.scalar.copy(v_hi[:, b, :], v_of[b]).then_inc(v_hi_done, 1)

            def split_v_tail(g, b):
                act.wait_ge(v_done, g * G + b + 1)
                nc.scalar.copy(v_hi[:, b, half:d], pair[b][:, BANK:BANK + w_tail]).then_inc(v_hi_done, 1)

            def split_v_head(b):
                act.wait_ge(v_head_done, b + 1)
                nc.scalar.copy(v_hi[:, b, 0:half], pair[b][:, v_from:BANK]).then_inc(v_head_hi_done, 1)

            def normalise(n, s, b0, b1, ends=True):
                act.wait_ge(offset_done, n)
                for b in range(b0, b1):
                    last = nc.scalar.activation(result[s][:, b, :], x_in[s][:, b, :], ACT.Identity,
                                                bias=offset[:, b:b + 1], scale=rstd[:, b:b + 1])
                if ends:
                    last.then_inc(normalised, 1)

            def group(g, s, use_next, first=False, last=False):
                if not last:
                    act.wait_ge(xt_loaded[1 - s], use_next * 16)
                    split_xt(1 - s, 0)
                    split_xt(1 - s, 1)
                split_y(g, 0)
                if not first:
                    exponent(g, 0, G)
                if not last:
                    split_xt(1 - s, 2)
                split_y(g, 1)
                if not first:
                    split_p(g, 0, G)
                if not last:
                    split_xt(1 - s, 3)
                split_y(g, 2)
                split_y(g, 3)
                if last:
                    return
                split_v(g, 0)
                if not first:
                    normalise(g, 1 - s, 0, 2, ends=False)
                split_v(g, 1)
                if not first:
                    normalise(g, 1 - s, 2, G)
                split_v(g, 2)
                split_v(g, 3)

            group(0, 0, 1, first=True)
            with act.Fori(0, groups // 2 - 1) as r:
                group(r * 2 + 1, 1, r + 2)
                group(r * 2 + 2, 0, r + 2)
            group(last_group, 1, 0, last=True)
            for b in range(3):
                split_v_tail(last_group, b)
            exponent(groups, *softmax_parts[0])
            split_v_tail(last_group, 3)
            normalise(last_group, 0, 0, 2, ends=False)
            split_p(groups, *softmax_parts[0])
            split_v_head(0)
            exponent(groups + 1, *softmax_parts[1])
            split_v_head(1)
            split_p(groups + 1, *softmax_parts[1])
            normalise(last_group, 0, 2, G)
            split_v_head(2)
            split_v_head(3)
            for n, part in enumerate(norm_parts):
                normalise(groups + n, 1, *part)

        @block.vector
        def _(dve):
            def split(lo, whole, hi):
                return nc.vector.tensor_tensor(lo, whole, hi.bitcast(F32), ALU.subtract)

            def split_xt(g, s, i):
                dve.wait_ge(xt_hi_done, g * chunks + i + 1)
                split(xt_lo[s][:, i, :], xt_in[s][:, i, :], xt_hi[s][:, i, :]).then_inc(xt_split, 1)

            for o in range(chunks):
                for n, (lo, whole, hi) in enumerate([(wq_lo, wqt_raw, wq_hi), (wk_lo, wkt_raw, wk_hi)]):
                    dve.wait_ge(wqk_hi_done, 2 * o + n + 1)
                    split(lo[:, o, :], whole[:, o, :], hi[:, o, :]).then_inc(wqk_split, 1)
            for i in range(chunks):
                split_xt(0, 0, i)
            for i in range(chunks):
                dve.wait_ge(m_hi_done, i + 1)
                split(m_lo[:, i, :], bank[4 + i], m_hi[:, i, :]).then_inc(m_split, 1)
            dve.wait_ge(w_hi_done, 1)
            split(w_lo[:, :, :], w_raw[:, :, 0:half], w_hi[:, :, :]).then_inc(w_split, 1)
            for b in range(G):
                dve.wait_ge(w_hi_done, b + 2)
                last_split = split(wy_lo[:, :, b, 0:w_tail], w_raw[:, :, half:d], wy_hi[:, :, b, 0:w_tail])
            last_split.then_inc(w_split, 1)

            def split_y(g, j):
                dve.wait_ge(y_hi_done, g * chunks + j + 1)
                split(wy_lo[:, j, :, w_tail:half], bank[j].rearrange("p (b n) -> p b n", b=G),
                      wy_hi[:, j, :, w_tail:half]).then_inc(y_split, 1)

            def split_v_and_mask(g, s, b):
                dve.wait_ge(v_hi_done, g * G + b + 1)
                split(v_lo[:, b, :], v_of[b], v_hi[:, b, :]).then_inc(v_split, 1)
                mask(s, b)

            def mask(s, b):
                c = slice(b * P, (b + 1) * P)
                nc.vector.scalar_tensor_tensor(out=masked[:, c], in0=adj_in[s][:, c], scalar=0.0,
                                               in1=alpha_of[b], op0=ALU.not_equal,
                                               op1=ALU.mult).then_inc(masked_done, 1)

            def split_v_tail_and_mask(b):
                dve.wait_ge(v_hi_done, last_group * G + b + 1)
                split(v_lo[:, b, half:d], pair[b][:, BANK:BANK + w_tail], v_hi[:, b, half:d]).then_inc(v_split, 1)
                mask(1, b)

            def split_v_head(b):
                dve.wait_ge(v_head_hi_done, b + 1)
                split(v_lo[:, b, 0:half], pair[b][:, v_from:BANK], v_hi[:, b, 0:half]).then_inc(v_head_split, 1)

            def by_batch(t, b0, b1):
                return t[:, b0 * P:b1 * P].rearrange("p (b n) -> p b n", b=b1 - b0)

            def over_n(t, b0, b1):
                return t[:, b0:b1].unsqueeze(2).to_broadcast([P, b1 - b0, nodes])

            def shift(n, masked_by, b0, b1):
                dve.wait_ge(masked_done, masked_by)
                nc.vector.reduce_max(row_max[:, b0:b1], by_batch(masked, b0, b1), AX_X).then_inc(max_done, 1)
                dve.wait_ge(max_done, n)
                nc.vector.tensor_scalar(row_max[:, b0:b1], row_max[:, b0:b1], 0.0, None,
                                        ALU.max).then_inc(clamp_done, 1)
                dve.wait_ge(clamp_done, n)
                nc.vector.scalar_tensor_tensor(out=by_batch(shifted, b0, b1), in0=by_batch(masked, b0, b1),
                                               scalar=0.0, in1=over_n(row_max, b0, b1), op0=ALU.max,
                                               op1=ALU.subtract).then_inc(shift_done, 1)

            def divide(n, b0, b1):
                dve.wait_ge(exp_done, n)
                nc.vector.reduce_sum(row_sum[:, b0:b1], by_batch(expd, b0, b1), AX_X).then_inc(sum_done, 1)
                dve.wait_ge(sum_done, n)
                nc.vector.reciprocal(row_inv[:, b0:b1], row_sum[:, b0:b1]).then_inc(inv_done, 1)
                dve.wait_ge(inv_done, n)
                nc.vector.tensor_tensor(by_batch(prob, b0, b1), by_batch(expd, b0, b1),
                                        over_n(row_inv, b0, b1), ALU.mult).then_inc(prob_done, 1)

            def split_p(n, b0, b1):
                c = slice(b0 * P, b1 * P)
                dve.wait_ge(p_hi_done, n)
                split(p_lo[:, c], prob[:, c], p_hi[:, c]).then_inc(p_split, 1)

            def residual(g, s, b, last_one):
                dve.wait_ge(attn_done, g * G + b + 1)
                nc.vector.tensor_tensor(x_in[s][:, b, :], attended(last_one, b), x_in[s][:, b, :],
                                        ALU.add).then_inc(residual_done, 1)

            def statistics(g, s, b):
                dve.wait_ge(residual_done, g * G + b + 1)
                nc.vector.bn_stats(stats[:, b, :], x_in[s][:, b, :]).then_inc(stats_done, 1)

            def moments(g, n, s, b0, b1, last_one=False):
                residual(g, s, b0, last_one)
                for b in range(b0 + 1, b1):
                    residual(g, s, b, last_one)
                    statistics(g, s, b - 1)
                statistics(g, s, b1 - 1)
                c = slice(b0, b1)
                mean_even, mean_odd = stats[:, c, 1], stats[:, c, 4]
                dve.wait_ge(stats_done, g * G + b1)
                nc.vector.tensor_tensor(mean_gap[:, c], mean_even, mean_odd, ALU.subtract)
                nc.vector.tensor_tensor(mean_sum[:, c], mean_even, mean_odd, ALU.add)
                nc.vector.tensor_tensor(square_sum[:, c], stats[:, c, 2], stats[:, c, 5],
                                        ALU.add).then_inc(halves_added, 1)
                dve.wait_ge(halves_added, n)
                nc.vector.scalar_tensor_tensor(out=gap_term[:, c], in0=mean_gap[:, c], scalar=0.25,
                                               in1=mean_gap[:, c], op0=ALU.mult, op1=ALU.mult)
                nc.vector.tensor_scalar(minus_mean[:, c], mean_sum[:, c], -0.5, None, ALU.mult)
                nc.vector.tensor_scalar(square_term[:, c], square_sum[:, c], 1.0 / d, EPS, ALU.mult,
                                        ALU.add).then_inc(terms_done, 1)
                dve.wait_ge(terms_done, n)
                nc.vector.tensor_tensor(var_eps[:, c], square_term[:, c], gap_term[:, c],
                                        ALU.add).then_inc(var_done, 1)

            def group(g, s, use, first=False, last=False):
                use_before = use if s == 1 else use - 1
                if not first:
                    split_v_and_mask(g - 1, 1 - s, G - 1)
                    shift(g, g * G, 0, G)
                split_y(g, 0)
                if not first:
                    divide(g, 0, G)
                split_y(g, 1)
                if not first:
                    split_p(g, 0, G)
                split_y(g, 2)
                if not last:
                    split_xt(g + 1, 1 - s, 0)
                    split_xt(g + 1, 1 - s, 1)
                split_y(g, 3)
                if not first:
                    dve.wait_ge(x_loaded[1 - s], use_before * 16)
                    moments(g - 1, g, 1 - s, 0, G)
                dve.wait_ge(adj_loaded[s], use * 16)
                if last:
                    return
                split_v_and_mask(g, s, 0)
                split_xt(g + 1, 1 - s, 2)
                split_xt(g + 1, 1 - s, 3)
                split_v_and_mask(g, s, 1)
                split_v_and_mask(g, s, 2)

            group(0, 0, 1, first=True)
            with dve.Fori(0, groups // 2 - 1) as r:
                group(r * 2 + 1, 1, r + 1)
                group(r * 2 + 2, 0, r + 2)
            group(last_group, 1, groups // 2, last=True)

            first_softmax, second_softmax = softmax_parts
            split_v_tail_and_mask(0)
            split_v_tail_and_mask(1)
            shift(groups, last_group * G + 2, *first_softmax)
            split_v_tail_and_mask(2)
            divide(groups, *first_softmax)
            split_v_tail_and_mask(3)
            shift(groups + 1, groups * G, *second_softmax)
            split_p(groups, *first_softmax)
            split_v_head(0)
            divide(groups + 1, *second_softmax)
            split_v_head(1)
            split_p(groups + 1, *second_softmax)
            split_v_head(2)
            dve.wait_ge(x_loaded[1], groups // 2 * 16)
            for n, part in enumerate(norm_parts):
                moments(last_group, groups + n, 1, *part, last_one=True)
                if n == 0:
                    split_v_head(3)

        @block.gpsimd
        def _(pool):
            nc.gpsimd.memset(minus_half[:, :], -0.5).then_inc(half_set, 1)
            nc.gpsimd.memset(zeros[:, :], 0.0).then_inc(zeros_set, 1)
            pool.wait_ge(half_set, 1)

            def root(n, b0, b1):
                c = slice(b0, b1)
                pool.wait_ge(var_done, n)
                nc.gpsimd.tensor_tensor(rstd[:, c], var_eps[:, c], minus_half[:, c], ALU.pow).then_inc(rstd_done, 1)
                pool.wait_ge(rstd_done, n)
                nc.gpsimd.tensor_tensor(offset[:, c], minus_mean[:, c], rstd[:, c], ALU.mult).then_inc(offset_done, 1)

            with pool.Fori(0, groups - 1) as g:
                root(g + 1, 0, G)
            for n, part in enumerate(norm_parts):
                root(groups + n, *part)


def kernel(x, adj, L0_gnn_weight, L0_gnn_wq, L0_gnn_wk):
    import numpy as np
    import concourse.bacc as bacc
    from concourse.bass_utils import run_bass_kernel_spmd

    x, adj = np.asarray(x), np.asarray(adj)
    batch, nodes, d = x.shape
    groups, chunks = batch // G, d // P

    def rows_in_chunks(m):
        m = np.asarray(m)
        return np.ascontiguousarray(m.reshape(chunks, P, m.shape[1]).transpose(1, 0, 2))

    arrays = {
        "xt": np.ascontiguousarray(x.reshape(groups, G, nodes, chunks, P).transpose(0, 4, 3, 1, 2)
                                   ).reshape(groups, P, chunks, G * nodes),
        "x": np.ascontiguousarray(x),
        "adjt": np.ascontiguousarray(adj.reshape(groups, G, nodes, nodes).transpose(0, 3, 1, 2)
                                     ).reshape(groups, nodes, G * nodes),
        "w": rows_in_chunks(L0_gnn_weight),
        "wqt": rows_in_chunks(np.asarray(L0_gnn_wq).T),
        "wkt": rows_in_chunks(np.asarray(L0_gnn_wk).T),
    }
    nc = bacc.Bacc("TRN2", target_bir_lowering=False, num_devices=1)
    args = {k: nc.dram_tensor(f"in_{k}", a.shape, mybir.dt.from_np(a.dtype), kind="ExternalInput").ap()
            for k, a in arrays.items()}
    out = nc.dram_tensor("out_y", x.shape, F32, kind="ExternalOutput").ap()
    graph_attention_layernorm(nc, **args, out=out)
    r = run_bass_kernel_spmd(nc, [{f"in_{k}": a for k, a in arrays.items()}], core_ids=[0])
    return r.results[0]["out_y"]
```
